# Optimizing a Trainium2 kernel written in Bass

```python
import numpy as np
import jax
import jax.numpy as jnp

def _softmax(x, axis=-1):
    return jax.nn.softmax(x, axis=axis)

def _gelu(x):
    return jax.nn.gelu(x, approximate=True)

def _silu(x):
    return jax.nn.silu(x)

def _sigmoid(x):
    return jax.nn.sigmoid(x)

def _layernorm(x, axis=-1, eps=1e-05):
    m = jnp.mean(x, axis=axis, keepdims=True)
    v = jnp.var(x, axis=axis, keepdims=True)
    return (x - m) / jnp.sqrt(v + eps)

def _scatter_add(tgt, idx, src, axis=0):
    return tgt.at[idx].add(src)

def _segment_sum(src, seg, n):
    return jax.ops.segment_sum(src, seg, n)
kernel_name = 'mk_decoder_preln_d1_seqx_r4_df1a2f'

def setup_inputs(seed: int=0):
    np.random.seed(seed)
    _w = jnp.asarray

    def _rec_inputs():
        import jax
        import jax.numpy as jnp
        _rk = jax.random.key(seed)
        x = -0.000125 + 0.9999 * jax.random.normal(jax.random.fold_in(_rk, 1), (2, 512, 1024), jnp.float32)
        _lenS = 512 - jax.random.randint(jax.random.fold_in(_rk, 7), (2,), 0, max(1, 512 // 4) + 1, jnp.int32)
        _lenS2 = 1024 - jax.random.randint(jax.random.fold_in(_rk, 8), (2,), 0, max(1, 1024 // 4) + 1, jnp.int32)
        _ctx_4096P = jax.random.normal(jax.random.fold_in(_rk, 11), (2, 16, 1024), jnp.float32)
        _ctx_4096c = jax.random.dirichlet(jax.random.fold_in(_rk, 511), 0.3 * jnp.ones((16,), jnp.float32), (2, 1024))
        _ctx_4096t = jnp.einsum('bsk,bkd->bsd', _ctx_4096c, _ctx_4096P)
        _ctx_4096t = _ctx_4096t * jax.lax.rsqrt(jnp.mean(jnp.square(_ctx_4096t)) + 1e-12) * 0.953939
        ctx_4096 = -5.72187e-05 + 0.999849 * (_ctx_4096t + 0.3 * jax.random.normal(jax.random.fold_in(_rk, 611), (2, 1024, 1024), jnp.float32))
        return (x, ctx_4096)
    x, ctx_4096 = _rec_inputs()

    def _L0_attn_setup():
        import jax, jax.numpy as jnp
        import numpy as np
        B, S, HID = (1, 512, 1024)
        H, HK, D = (32, 8, 128)
        L = D // 4
        key = jax.random.key(seed)
        ks = jax.random.split(key, 7)
        s = 0.02
        return {'hidden_states': jax.random.normal(ks[0], (B, S, HID), jnp.float32), 'Wq': jax.random.normal(ks[1], (H * D, HID), jnp.float32) * s, 'Wk_down': jax.random.normal(ks[2], (HK * L, HID), jnp.float32) * s, 'Wv_down': jax.random.normal(ks[3], (HK * L, HID), jnp.float32) * s, 'Wk_up': jax.random.normal(ks[4], (HK * D, HK * L), jnp.float32) * s, 'Wv_up': jax.random.normal(ks[5], (HK * D, HK * L), jnp.float32) * s, 'Wo': jax.random.normal(ks[6], (HID, H * D), jnp.float32) * s}
    _L0_attn_all = _L0_attn_setup()
    _L0_attn_in = {k: v for k, v in _L0_attn_all.items() if k in ('Wq', 'Wk_down', 'Wv_down', 'Wk_up', 'Wv_up', 'Wo')}
    del _L0_attn_all

    def _L0_xattn_setup():
        import jax, jax.numpy as jnp
        import numpy as np
        QMIN = 0.0
        QMAX = 255.0

        def fake_quant(x, scale, zp):
            s = scale.reshape(())
            z = zp.reshape(())
            q = jnp.clip(jnp.round(x / s + z), QMIN, QMAX)
            return (q - z) * s
        key = jax.random.key(seed)
        k1, k2 = jax.random.split(key)
        B, M, K, N = (4, 512, 1024, 1024)
        x1 = jax.random.normal(k1, (B, M, K), dtype=jnp.float32)
        x2 = jax.random.normal(k2, (B, K, N), dtype=jnp.float32)
        x1_scale = jnp.full((1,), 8.0 / 255.0, dtype=jnp.float32)
        x1_zp = jnp.full((1,), 128.0, dtype=jnp.float32)
        x2_scale = jnp.full((1,), 8.0 / 255.0, dtype=jnp.float32)
        x2_zp = jnp.full((1,), 128.0, dtype=jnp.float32)
        return {'x1': x1, 'x2': x2, 'x1_scale': x1_scale, 'x1_zp': x1_zp, 'x2_scale': x2_scale, 'x2_zp': x2_zp}
    _L0_xattn_all = _L0_xattn_setup()
    _L0_xattn_in = {k: v for k, v in _L0_xattn_all.items() if k in ('x1_scale', 'x1_zp', 'x2_scale', 'x2_zp')}
    del _L0_xattn_all

    def _L0_ffn_setup():
        import jax, jax.numpy as jnp
        import numpy as np
        IN_F = 1024
        OUT_F = 1024
        RANK = 8
        NUM_EXPERTS = 64
        TOP_K = 16
        ROUTER_DIM = 16
        ALPHA = 32
        SCALING = ALPHA / TOP_K
        BOTTLENECK = NUM_EXPERTS * RANK
        key = jax.random.key(seed)
        ks = jax.random.split(key, 5)
        x = jax.random.normal(ks[0], (4, 1024, IN_F), dtype=jnp.float32)
        bound_a = float(np.sqrt(6.0 / IN_F))
        A_w = jax.random.uniform(ks[1], (BOTTLENECK, IN_F), jnp.float32, -bound_a, bound_a)
        B_w = jax.random.normal(ks[2], (OUT_F, BOTTLENECK), dtype=jnp.float32) * 0.02
        Wq_w = jax.random.normal(ks[3], (ROUTER_DIM, IN_F), dtype=jnp.float32) * 0.02
        keys = jax.random.normal(ks[4], (NUM_EXPERTS, ROUTER_DIM), dtype=jnp.float32) * 0.01
        return {'x': x, 'A_w': A_w, 'B_w': B_w, 'Wq_w': Wq_w, 'keys': keys}
    _L0_ffn_all = _L0_ffn_setup()
    _L0_ffn_in = {k: v for k, v in _L0_ffn_all.items() if k in ('A_w', 'B_w', 'Wq_w', 'keys')}
    del _L0_ffn_all
    return {'x': x, 'ctx_4096': ctx_4096, 'L0_attn_Wq': _L0_attn_in['Wq'], 'L0_attn_Wk_down': _L0_attn_in['Wk_down'], 'L0_attn_Wv_down': _L0_attn_in['Wv_down'], 'L0_attn_Wk_up': _L0_attn_in['Wk_up'], 'L0_attn_Wv_up': _L0_attn_in['Wv_up'], 'L0_attn_Wo': _L0_attn_in['Wo'], 'L0_xattn_x1_scale': _L0_xattn_in['x1_scale'], 'L0_xattn_x1_zp': _L0_xattn_in['x1_zp'], 'L0_xattn_x2_scale': _L0_xattn_in['x2_scale'], 'L0_xattn_x2_zp': _L0_xattn_in['x2_zp'], 'L0_ffn_A_w': _L0_ffn_in['A_w'], 'L0_ffn_B_w': _L0_ffn_in['B_w'], 'L0_ffn_Wq_w': _L0_ffn_in['Wq_w'], 'L0_ffn_keys': _L0_ffn_in['keys']}

def reference(x, ctx_4096, L0_attn_Wq, L0_attn_Wk_down, L0_attn_Wv_down, L0_attn_Wk_up, L0_attn_Wv_up, L0_attn_Wo, L0_xattn_x1_scale, L0_xattn_x1_zp, L0_xattn_x2_scale, L0_xattn_x2_zp, L0_ffn_A_w, L0_ffn_B_w, L0_ffn_Wq_w, L0_ffn_keys):
    import jax
    import jax.numpy as jnp

    def _L0_attn_ref(hidden_states, Wq, Wk_down, Wv_down, Wk_up, Wv_up, Wo):
        import jax, jax.numpy as jnp
        import numpy as np
        B, S, HID = (1, 512, 1024)
        H, HK, D = (32, 8, 128)
        L = D // 4
        b, s, _ = hidden_states.shape
        q = (hidden_states @ Wq.T).reshape(b, s, H, D).transpose(0, 2, 1, 3)
        kc = (hidden_states @ Wk_down.T).reshape(b, s, HK, L).transpose(0, 2, 1, 3)
        vc = (hidden_states @ Wv_down.T).reshape(b, s, HK, L).transpose(0, 2, 1, 3)
        lat = jnp.concatenate([kc, vc], axis=-1).reshape(b, s, HK * 2 * L)
        k_cmp, v_cmp = jnp.split(lat, 2, axis=-1)
        k = (k_cmp @ Wk_up.T).reshape(b, s, HK, D).transpose(0, 2, 1, 3)
        v = (v_cmp @ Wv_up.T).reshape(b, s, HK, D).transpose(0, 2, 1, 3)
        n_rep = H // HK
        k = jnp.repeat(k, n_rep, axis=1)
        v = jnp.repeat(v, n_rep, axis=1)
        scale = 1.0 / jnp.sqrt(jnp.asarray(D, hidden_states.dtype))
        scores = jnp.einsum('bhqd,bhkd->bhqk', q, k) * scale
        causal = jnp.tril(jnp.ones((s, s), dtype=bool))
        scores = jnp.where(causal, scores, jnp.asarray(-1000000000.0, scores.dtype))
        attn = jax.nn.softmax(scores, axis=-1)
        out = jnp.einsum('bhqk,bhkd->bhqd', attn, v)
        out = out.transpose(0, 2, 1, 3).reshape(b, s, H * D)
        return out @ Wo.T

    def _L0_xattn_ref(x1, x2, x1_scale, x1_zp, x2_scale, x2_zp):
        import jax, jax.numpy as jnp
        import numpy as np
        QMIN = 0.0
        QMAX = 255.0

        def fake_quant(x, scale, zp):
            s = scale.reshape(())
            z = zp.reshape(())
            q = jnp.clip(jnp.round(x / s + z), QMIN, QMAX)
            return (q - z) * s
        q1 = fake_quant(x1, x1_scale, x1_zp)
        q2 = fake_quant(x2, x2_scale, x2_zp)
        return jnp.matmul(q1, q2)

    def _L0_ffn_ref(x, A_w, B_w, Wq_w, keys):
        import jax, jax.numpy as jnp
        import numpy as np
        IN_F = 1024
        OUT_F = 1024
        RANK = 8
        NUM_EXPERTS = 64
        TOP_K = 16
        ROUTER_DIM = 16
        ALPHA = 32
        SCALING = ALPHA / TOP_K
        BOTTLENECK = NUM_EXPERTS * RANK
        q = jnp.einsum('bsd,rd->bsr', x, Wq_w)
        scores = jnp.einsum('bsr,er->bse', q, keys)
        top_vals, top_idx = jax.lax.top_k(scores, TOP_K)
        top_w = jax.nn.softmax(top_vals, axis=-1)
        gate = jnp.sum(jax.nn.one_hot(top_idx, NUM_EXPERTS, dtype=top_w.dtype) * top_w[..., None], axis=-2)
        z = jnp.einsum('bsd,nd->bsn', x, A_w)
        z = z.reshape(*z.shape[:-1], NUM_EXPERTS, RANK)
        z_gated = (z * gate[..., None]).reshape(*z.shape[:-2], BOTTLENECK)
        out = jnp.einsum('bsn,on->bso', z_gated, B_w) * SCALING
        return out
    x = x + _L0_attn_ref(_layernorm(x, axis=-1), L0_attn_Wq, L0_attn_Wk_down, L0_attn_Wv_down, L0_attn_Wk_up, L0_attn_Wv_up, L0_attn_Wo)
    x = x + _L0_xattn_ref(_layernorm(x, axis=-1), ctx_4096, L0_xattn_x1_scale, L0_xattn_x1_zp, L0_xattn_x2_scale, L0_xattn_x2_zp)
    x = x + _L0_ffn_ref(_layernorm(x, axis=-1), L0_ffn_A_w, L0_ffn_B_w, L0_ffn_Wq_w, L0_ffn_keys)
    return x

_drawn_inputs = setup_inputs


def setup_inputs(seed=0):
    import zlib

    import numpy as np

    out = dict(_drawn_inputs(seed))
    spreads = {}
    factors = {'L0_attn_Wq': 7.002,
     'L0_attn_Wk_up': 6.804,
     'L0_ffn_A_w': 8.0,
     'L0_ffn_B_w': 8.0,
     'L0_ffn_Wq_w': 8.0,
     'L0_ffn_keys': 8.0}
    for name, (base, spread) in spreads.items():
        noise = np.random.default_rng([zlib.crc32(name.encode()), seed]).standard_normal(out[name].shape)
        drawn = base * np.exp(spread * noise) if base else spread * noise
        out[name] = jnp.asarray(drawn.astype(out[name].dtype))
    for name, factor in factors.items():
        out[name] = (out[name] * factor).astype(out[name].dtype)
    return out
```

```python
from contextlib import ExitStack

import concourse.bass as bass
from concourse import mybir

ALU = mybir.AluOpType
ACT = mybir.ActivationFunctionType
F32 = mybir.dt.float32
F16 = mybir.dt.float16
BF16 = mybir.dt.bfloat16

P = 128
BATCH, SEQ, DIM = 2, 512, 1024
TOK = BATCH * SEQ
TT = TOK // P
KT = DIM // P
HEADS, KV_HEADS, HD = 32, 8, 128
GROUP = HEADS // KV_HEADS
LAT = HD // 4
QT = SEQ // P
HALF = 512
CTX_K, CTX_N = 1024, 1024
EXPERTS, RANK, TOP_K, ROUTER = 64, 8, 16, 16
BOTTLE = EXPERTS * RANK
BT = BOTTLE // P
EPS = 1e-5

S_H = 2.0 ** 8
S_W = 2.0 ** 8
S_LAT = 2.0 ** 6
S_K = 2.0 ** 4
S_V = 2.0 ** 6
S_Q = 2.0 ** 4
S_P = 2.0 ** 8
S_O = 2.0 ** 6
LAT_OUT = S_LAT / (S_H * S_W)
K_OUT = S_K / (S_LAT * S_W)
V_OUT = S_V / (S_LAT * S_W)
Q_OUT = S_Q / (S_H * S_W)
O_OUT = S_O / (S_P * S_V)
WO_OUT = 1.0 / (S_O * S_W)
SOFTMAX = HD ** -0.5 / (S_Q * S_K)
MASKED = -1.0e30

S_AT = {2: 0, 0: 3 * P, 3: 4 * P, 1: 8 * P}
S_BANKS = ((2, 0), (3,), (1,))
S_COLS = 10 * P
PT_AT = {0: 0, 1: 4 * P, 3: 7 * P, 2: 8 * P}
PT_TURNS = ((0,), (1, 3), (2,))
PT_BANK = (3, 4, 3)
PV_BANK = 5
GEN_BANK = (6, 7)
DOWN_BANK = (4, 5, 6, 7)
FIRST_Q, FIRST_K, FIRST_V = (0, 1), (2, 3), (6, 7)
PAIRS = TT // 2

S_Z = 2.0 ** 4
Z_OUT = S_Z / (S_H * S_W)
ROUTER_OUT = 1.0 / (S_H * S_W)
FFN_OUT = (32 / TOP_K) / (S_Z * S_W)
ROUND = 2.0 ** 23
CENTRE = 128.0
QMAX = 255.0
TAKEN = -3.0e38
CTX_CHUNKS = BATCH * CTX_K // P
TURN_BANK = 0
X_BANK = (1, 2)
H_BANK = (3, 4)
Z_BANK = 5
SMALL_BANK = 6
ZT_BANK = 7
COLUMN_BANK = (X_BANK, (Z_BANK, ZT_BANK))
R_COL, S_COL, SUM_COL = 0, P, P + EXPERTS
STEPS_AHEAD = 2

LAST_BANKS = 8

UNITS = GROUP * BATCH
STEPS = UNITS + 2
WO_CHUNKS = 2 * TT
LEAD = 2
DOWN = 4


def bank_uses(last):
    order = []
    for u in range(STEPS):
        if u < UNITS and not (last and u + LEAD >= UNITS):
            order.append(("q", u + LEAD))
        if u == UNITS and not last:
            order += [("k", b) for b in range(BATCH)]
        if u >= UNITS - 2:
            order += [("wo", 0, c) for c in wo_span(u)]
    if not last:
        order += [("v", b) for b in range(BATCH)]
    order += [("wo", 1, c) for c in range(WO_CHUNKS)]
    return {what: n for n, what in enumerate(order)}


def wo_span(u):
    return range(4 * (u - UNITS + 2), 4 * (u - UNITS + 3))


def side_steps(first):
    if first:
        return [("b", n, n + 1, n + 1) for n in range(BT)] + [("ctx", 0, 5, 6), ("ctx", 1, 7, 8)]
    return [("ctx", 0, 1, 2), ("ctx", 1, 5, 6)]


def side_number(g, first, n):
    return n if first else BT + 2 * g + n


USES = {last: bank_uses(last) for last in (False, True)}
PER_GROUP = len(USES[False])
PRE_USES = 2 * DOWN + 2 * BATCH + LEAD
HI_PER_GROUP = UNITS + 2 * BATCH
PRE_HI = PRE_USES


def decoder_layer(nc, x, ctx_in, wq, wdown, wup, wo, a_w, b_w, router_w, keys, quant, ctx_whole, out):
    ctx = ExitStack()

    def sb(name, shape, dt):
        return ctx.enter_context(nc.sbuf_tensor(name, shape, dt))

    def sem(name):
        return ctx.enter_context(nc.semaphore(name))

    with ctx:
        ps = ctx.enter_context(nc.psum_tensor("ps", [P, 8, HALF], F32))
        x_sb = sb("x_sb", [P, TT, DIM], F32)
        h_t = sb("h_t", [P, 2, KT, TOK], F16)
        lat = sb("lat", [P, 2, 4, TOK], F16)
        k_t = sb("k_t", [P, 2, TOK], F16)
        v_sb = sb("v_sb", [P, 2, BATCH, QT, HD], F16)
        up_in = sb("up_in", [P, 2, 2, HD], F32)
        up = sb("up", [P, 2, 2, 2, HD], F16)
        wq_in = sb("wq_in", [P, 2, KT * HD], F32)
        wq_sb = sb("wq_sb", [P, 2, 2, KT * HD], F16)
        wo_in = sb("wo_in", [P, 2, DIM], F32)
        wo_sb = sb("wo_sb", [P, GROUP, 2, DIM], F16)
        q_t = sb("q_t", [P, 4, 2, SEQ], F16)
        prob = sb("prob", [P, 2, S_COLS], F32)
        prob_t = sb("prob_t", [P, 2, 2, S_COLS], F16)
        o_t = sb("o_t", [P, GROUP, 2, TOK], F16)
        mask = sb("mask", [P, SEQ], F32)
        ident = sb("ident", [P, P], F32)
        row_max = sb("row_max", [P, 2, QT], F32)
        neg_max = sb("neg_max", [P, 2, QT], F32)
        row_sum = sb("row_sum", [P, 2, QT], F32)
        row_inv = sb("row_inv", [P, 2, QT], F32)
        stats = sb("stats", [P, 3 * TT, 2, 6], F32)
        mean_var = sb("mean_var", [P, 3 * TT, 2], F32)
        var_eps = sb("var_eps", [P, 3 * TT], F32)
        rstd0 = sb("rstd0", [P, 3 * TT], F32)
        rstd1 = sb("rstd1", [P, 3, 3 * TT], F32)
        ident_b = sb("ident_b", [P, P], BF16)
        minus_half = sb("minus_half", [P, 1], F32)

        b_sb = sb("b_sb", [P, 2, BT, DIM], F16)
        side_in = sb("side_in", [P, CTX_N], F32)
        side_out = sb("side_out", [P, 2, CTX_N], BF16)
        router_in = sb("router_in", [P, KT * ROUTER], F32)
        router_sb = sb("router_sb", [P, KT, 2, ROUTER], F16)
        keys_sb = sb("keys_sb", [2 * ROUTER, EXPERTS], F32)
        quant_sb = sb("quant_sb", [P, 4], F32)
        inv_scale = sb("inv_scale", [P, 2], F32)
        both_scales = sb("both_scales", [P, 1], F32)
        shift = sb("shift", [P, 2], F32)
        shift_scaled = sb("shift_scaled", [P, 3], F32)
        ones = sb("ones", [P, P], BF16)
        row_term = sb("row_term", [P, TT], F32)
        best = sb("best", [P, 2, 2, 8], F32)
        neg_best = sb("neg_best", [P, 2], F32)
        gate_sum = sb("gate_sum", [P, TT], F32)
        gate_inv = sb("gate_inv", [P, TT], F32)
        gate_scale = sb("gate_scale", [P, TT], F32)
        a_sb = lat
        spare = up[:, :, :, :, :].rearrange("p a b c d -> p (a b c d)").bitcast(F32)
        score, weight, gate = (spare[:, n * P:(n + 1) * P].rearrange("p (a e) -> p a e", a=2) for n in range(3))
        left = mask[:, 0:4 * EXPERTS].rearrange("p (a b e) -> p a b e", a=2, b=2)
        r_q = mask[0:2 * ROUTER, 2 * P:4 * P].rearrange("p (a n) -> p a n", a=2)
        ctx_q = h_t[:, :, :, :].bitcast(BF16)
        x_q = prob_t[:, :, 0, 0:DIM].bitcast(BF16)
        x_qt = q_t[:, 0:2, :, :].rearrange("p a b c -> p a (b c)").bitcast(BF16)
        z_t = q_t[:, 2:4, :, :].rearrange("p a b c -> p a b c")
        h3 = (k_t[:, :, :].rearrange("p a b -> p (a b)").bitcast(F32),
              v_sb[:, :, :, :, :].rearrange("p a b c d -> p (a b c d)").bitcast(F32))
        h3_t = wq_sb
        gated = up_in[:, :, :, :].rearrange("p a b c -> p (a b c)")
        column_term = wo_in
        down_in = o_t[:, :, :, :].rearrange("p a b c -> p a (b c)").bitcast(F32)

        quant_loaded = sem("quant_loaded")
        router_loaded = sem("router_loaded")
        side_loaded = sem("side_loaded")
        ctx_stored = sem("ctx_stored")
        ctx_loaded = [sem(f"ctx_loaded{n}") for n in range(BATCH)]
        x_loaded = [sem(f"x_loaded{n}") for n in range(TT)]
        wq_loaded = [sem(f"wq_loaded{n}") for n in range(2)]
        down_loaded = [sem(f"down_loaded{n}") for n in range(DOWN)]
        wo_loaded = [sem(f"wo_loaded{n}") for n in range(2)]
        up_loaded = sem("up_loaded")
        stored = sem("stored")
        consts = sem("consts")
        pow_done = sem("pow_done")
        prob_normed = sem("prob_normed")
        var_done = sem("var_done")
        newton = sem("newton")
        ln_done = sem("ln_done")
        ht_lo = sem("ht_lo")
        wq_lo = sem("wq_lo")
        wo_lo = sem("wo_lo")
        up_lo = sem("up_lo")
        gen_read = sem("gen_read")
        max_done = sem("max_done")
        scores_read = sem("scores_read")
        inv_done = sem("inv_done")
        pt_lo = sem("pt_lo")
        o_lo = sem("o_lo")
        ht_hi = sem("ht_hi")
        wq_hi = sem("wq_hi")
        down_scaled = sem("down_scaled")
        wo_hi = sem("wo_hi")
        up_hi = sem("up_hi")
        gen_hi = sem("gen_hi")
        exp_done = sem("exp_done")
        pt_hi = sem("pt_hi")
        o_hi = sem("o_hi")
        sp_passed = sem("sp_passed")
        pool_passed = sem("pool_passed")
        dve_passed = sem("dve_passed")
        ctx_clipped = sem("ctx_clipped")
        ctx_affine = sem("ctx_affine")
        side_hi = sem("side_hi")
        x_affine = sem("x_affine")
        x_qt_copied = sem("x_qt_copied")
        h3_hi = sem("h3_hi")
        router_hi = sem("router_hi")
        r_copied = sem("r_copied")
        s_copied = sem("s_copied")
        weighted = sem("weighted")
        zt_hi = sem("zt_hi")
        side_read = sem("side_read")
        ln2_done = sem("ln2_done")
        x_rounded = sem("x_rounded")
        row_read = sem("row_read")
        column_read = sem("column_read")
        x_added = sem("x_added")
        h3_done = sem("h3_done")
        h3_lo = sem("h3_lo")
        router_lo = sem("router_lo")
        best_done = sem("best_done")
        z_gated = sem("z_gated")
        zt_lo = sem("zt_lo")
        out_done = sem("out_done")
        x_turned = sem("x_turned")
        column_done = sem("column_done")
        rows_done = sem("rows_done")
        x_done = sem("x_done")
        h3_turned = sem("h3_turned")
        r_done = sem("r_done")
        z_done = sem("z_done")
        s_done = sem("s_done")
        z_turned = sem("z_turned")
        out_full = sem("out_full")
        ln_turned = sem("ln_turned")
        scores_done = sem("scores_done")
        pt_done = sem("pt_done")
        pv_done = sem("pv_done")
        gen_done = sem("gen_done")

        hn = prob[:, :, 0:DIM]

        def gen_number(g, last, what):
            return PRE_USES + g * PER_GROUP + USES[last][what] + 1

        def hi_number(g, last, what):
            earlier = [w for w, n in USES[last].items() if w[0] != "wo" and n <= USES[last][what]]
            return PRE_HI + g * HI_PER_GROUP + len(earlier)

        def latent_views(b, hp, half, j):
            bank = ps[:, DOWN_BANK[hp], :]
            src = bank[64 * half:64 * half + 64, :].rearrange("p (t i j) -> p i j t", i=4, j=2)[:, :, j, :]
            at = b * SEQ + 64 * (2 * hp + half)
            return src, [lat[64 * j:64 * j + 64, part, :, at:at + 64] for part in range(2)]

        def down_heads(t):
            return (0,) if t == 5 else (1, 2, 3)

        block = ctx.enter_context(nc.Block())

        @block.sync
        def _(sp):
            sp.dma_start(x_sb[:, 0, :], x[0]).then_inc(x_loaded[0], 16)
            for n in range(DOWN):
                sp.dma_start(x_sb[:, n + 1, :], x[n + 1]).then_inc(x_loaded[n + 1], 16)
                sp.dma_start(down_in[:, n, :], wdown[n]).then_inc(down_loaded[n], 16)
            for t in range(DOWN + 1, TT):
                sp.dma_start(x_sb[:, t, :], x[t]).then_inc(x_loaded[t], 16)
            sp.dma_start(up_in[:, :, :, :], wup[0]).then_inc(up_loaded, 16)
            sp.dma_start(quant_sb[:, :], quant[0, :].partition_broadcast(P)).then_inc(quant_loaded, 16)
            sp.dma_start(router_in[:, :], router_w[:, :]).then_inc(router_loaded, 16)
            for n in range(2):
                sp.dma_start(keys_sb[n * ROUTER:(n + 1) * ROUTER, :], keys[:, :]).then_inc(router_loaded, 16)
            for n in range(2):
                sp.dma_start(wq_in[:, n, :], wq[n]).then_inc(wq_loaded[n], 16)

            def load_wq(h):
                j = h[1] % 2
                sp.wait_ge(wq_lo, 4 * h[0] + h[1] - 1)
                sp.dma_start(wq_in[:, j, :], wq[4 * h[0] + h[1]]).then_inc(wq_loaded[j], 16)

            def load_wo(h):
                j = h[1] % 2
                sp.wait_ge(wo_lo, DOWN + 4 * h[0] + h[1] - 1)
                sp.dma_start(wo_in[:, j, :], wo[4 * h[0] + h[1]]).then_inc(wo_loaded[j], 16)

            def load_a(n):
                sp.wait_ge(wq_lo, HEADS + n - 1)
                sp.dma_start(wq_in[:, n % 2, :], a_w[:, n, :]).then_inc(wq_loaded[n % 2], 16)

            def load_side(g, first, n, src):
                if not (first and n == 0):
                    sp.wait_ge(side_read, side_number(g, first, n))
                    sp.sem_inc(sp_passed)
                sp.dma_start(side_in[:, :], src).then_inc(side_loaded, 16)

            def store_ctx(g, first, n):
                sp.wait_ge(side_read, side_number(g, first, BT + n if first else n) + 1)
                sp.sem_inc(sp_passed)
                sp.dma_start(ctx_whole[2 * g + n], side_out[:, n, :]).then_inc(ctx_stored, 16)

            def load_ctx(b):
                sp.wait_ge(gen_done, gen_number(KV_HEADS - 1, True, ("q", UNITS - 1)))
                sp.wait_ge(ctx_stored, 16 * KT * (b + 1))
                sp.dma_start(ctx_q[:, b, :, :], ctx_whole[b * KT:(b + 1) * KT].rearrange("c p n -> p c n"))\
                    .then_inc(ctx_loaded[b], 16)

            def first_group():
                load_wq((0, 2))
                load_wo((0, 0))
                load_side(0, True, 0, b_w[:, 0, :])
                load_wq((0, 3))
                load_side(0, True, 1, b_w[:, 1, :])
                load_wo((0, 1))
                load_side(0, True, 2, b_w[:, 2, :])
                load_wq((0, 4))
                load_side(0, True, 3, b_w[:, 3, :])
                load_wo((0, 2))
                load_side(0, True, BT, ctx_in[0])
                load_wq((0, 5))
                load_wo((0, 3))
                load_up(0)
                store_ctx(0, True, 0)
                load_side(0, True, BT + 1, ctx_in[1])
                store_ctx(0, True, 1)

            def load_up(g):
                sp.wait_ge(up_lo, g + 1)
                sp.dma_start(up_in[:, :, :, :], wup[g + 1]).then_inc(up_loaded, 16)

            def group(g, last):
                load_wq((g, 2))
                load_wo((g, 0))
                load_side(g, False, 0, ctx_in[2 * g])
                load_wq((g, 3))
                load_wo((g, 1))
                store_ctx(g, False, 0)
                load_side(g, False, 1, ctx_in[2 * g + 1])
                if last:
                    load_a(0)
                    load_wo((g, 2))
                    load_a(1)
                    load_wo((g, 3))
                    load_a(2)
                    load_a(3)
                    load_ctx(0)
                    store_ctx(g, False, 1)
                    load_ctx(1)
                else:
                    load_wq((g, 4))
                    load_wo((g, 2))
                    load_wq((g, 5))
                    load_wo((g, 3))
                    load_up(g)
                    store_ctx(g, False, 1)

            first_group()
            with sp.Fori(1, KV_HEADS - 1) as g:
                group(g, False)
            group(KV_HEADS - 1, True)
            for t in range(TT):
                sp.wait_ge(out_done, 2 * t + 2)
                sp.dma_start(out[t], x_sb[:, t, :]).then_inc(stored, 16)
            sp.wait_ge(stored, 16 * TT)

        @block.gpsimd
        def _(pool):
            nc.gpsimd.memset(ident[:, :], 0.0).then_inc(consts, 1)
            nc.gpsimd.memset(mask[:, :], 0.0).then_inc(consts, 1)
            nc.gpsimd.memset(minus_half[:, :], -0.5).then_inc(consts, 1)
            nc.gpsimd.memset(ones[:, :], 1.0).then_inc(consts, 1)
            pool.wait_ge(consts, 4)
            nc.gpsimd.affine_select(out=ident[:, :], in_=ident[:, :], compare_op=ALU.not_equal, fill=1.0,
                                    base=0, pattern=[[-1, P]], channel_multiplier=1).then_inc(consts, 1)
            nc.gpsimd.affine_select(out=mask[:, SEQ - P:SEQ], in_=mask[:, SEQ - P:SEQ], compare_op=ALU.is_ge,
                                    fill=MASKED, base=0, pattern=[[-1, P]], channel_multiplier=1).then_inc(consts, 1)
            for t in range(TT):
                pool.wait_ge(var_done, t + 1)
                nc.gpsimd.tensor_tensor(rstd0[:, t:t + 1], var_eps[:, t:t + 1], minus_half[:, :],
                                        ALU.pow).then_inc(pow_done, 1)
                if 2 <= t < DOWN + 2:
                    n = t - 2
                    pool.wait_ge(wo_hi, n + 1)
                    nc.gpsimd.tensor_tensor(wo_sb[:, n, 1, :], down_in[:, n, :], wo_sb[:, n, 0, :],
                                            ALU.subtract).then_inc(wo_lo, 1)

            def clip(number):
                pool.wait_ge(ctx_affine, number + 1)
                pool.sem_inc(pool_passed)
                nc.gpsimd.tensor_scalar(side_in[:, :], side_in[:, :], QMAX, 0.0, ALU.min, ALU.max)\
                    .then_inc(ctx_clipped, 1)

            def group(g):
                first = isinstance(g, int) and g == 0
                for u in range(UNITS):
                    pool.wait_ge(inv_done, UNITS * g + u + 1)
                    pool.sem_inc(pool_passed)
                    for q in range(QT):
                        at = prob[:, u % 2, S_AT[q]:S_AT[q] + (q + 1) * P]
                        ins = nc.gpsimd.tensor_scalar(at, at, row_inv[:, u % 2, q:q + 1], S_P, ALU.mult, ALU.mult)
                    ins.then_inc(prob_normed, 1)
                    for what, n, step, _ in side_steps(first):
                        if what == "ctx" and step == u:
                            clip(2 * g + n)

            group(0)
            with pool.Fori(1, KV_HEADS) as g:
                group(g)

            n = TT
            for i in range(-STEPS_AHEAD, TT):
                for t, k in ((i, 2), (i + STEPS_AHEAD, 1)):
                    if 0 <= t < TT:
                        n += 1
                        pool.wait_ge(var_done, n)
                        nc.gpsimd.tensor_tensor(rstd0[:, k * TT + t:k * TT + t + 1], var_eps[:, k * TT + t:k * TT + t + 1],
                                                minus_half[:, :], ALU.pow).then_inc(pow_done, 1)

        @block.scalar
        def _(act):
            def split_hi(dst, src, signal, scale):
                nc.scalar.activation(dst, src, ACT.Copy, scale=scale).then_inc(signal, 1)

            def wq_split(g, n):
                j = n % 2
                act.wait_ge(wq_loaded[j], 16 * (2 * g + n // 2 + 1))
                if not (isinstance(g, int) and g == 0 and n < 2):
                    g0, n0 = (g, n - 2) if n >= 2 else (g - 1, n + 2)
                    if n >= 4:
                        act.wait_ge(gen_done, gen_number(g, False, ("q", 2 * n - 3)))
                    elif isinstance(g, int) and g == 0 and n == 2:
                        act.wait_ge(gen_done, 2 * DOWN + LEAD)
                    elif n == 2:
                        act.wait_ge(gen_done, PRE_USES + (g - 1) * PER_GROUP + USES[False][("q", 9)] + 1)
                    else:
                        act.wait_ge(gen_done, gen_number(g, False, ("q", 3)))
                split_hi(wq_sb[:, j, 0, :], wq_in[:, j, :], wq_hi, S_W)

            def wo_split(g, n):
                act.wait_ge(wo_loaded[n % 2], 16 * (2 * g + n // 2 + 1))
                if isinstance(g, int) and g == 0:
                    act.wait_ge(gen_done, 2 * DOWN)
                else:
                    act.wait_ge(gen_done, PRE_USES + (g - 1) * PER_GROUP + USES[False][("wo", n // 2, WO_CHUNKS - 1)] + 1)
                split_hi(wo_sb[:, n, 0, :], wo_in[:, n % 2, :], wo_hi, S_W)

            def columns_hi(t):
                for j in range(2):
                    act.wait_ge(ln_turned, 2 * t + j + 1)
                    split_hi(h_t[:, 0, 4 * j:4 * j + 4, t * P:(t + 1) * P],
                             ps[:, 2 * (t % 2) + j, :].rearrange("p (k n) -> p k n", k=4), ht_hi, S_H)

            def latent_hi(b, hp):
                act.wait_ge(gen_done, b * DOWN + hp + 1)
                for half in range(2):
                    for j in range(2):
                        src, (hi, _) = latent_views(b, hp, half, j)
                        ins = nc.scalar.activation(hi, src, ACT.Copy, scale=LAT_OUT)
                ins.then_inc(gen_hi, 1)

            for t in range(TT):
                if t in (5, 6):
                    for hp in down_heads(t):
                        latent_hi(0, hp)
                columns_hi(t)
                if t < DOWN:
                    act.wait_ge(down_loaded[t], 16)
                    split_hi(down_in[:, t, :], down_in[:, t, :], down_scaled, S_W)
                    act.wait_ge(down_scaled, t + 1)
                    split_hi(wo_sb[:, t, 0, :], down_in[:, t, :], wo_hi, 1.0)
            for n in range(2):
                act.wait_ge(wq_loaded[n], 16)
                split_hi(wq_sb[:, n, 0, :], wq_in[:, n, :], wq_hi, S_W)
            act.wait_ge(up_loaded, 16)
            split_hi(up[:, 0, :, :, :], up_in[:, :, :, :], up_hi, S_W)
            act.wait_ge(router_loaded, 48)
            split_hi(router_sb[:, :, 0, :], router_in[:, :].rearrange("p (k r) -> p k r", r=ROUTER), router_hi, S_W)

            for hp in range(DOWN):
                latent_hi(1, hp)

            def a_split(n):
                act.wait_ge(wq_loaded[n % 2], 16 * (HEADS // 2 + n // 2 + 1))
                split_hi(a_sb[:, 0, n, :], wq_in[:, n % 2, :], wq_hi, S_W)

            def side_work(g, first, u):
                for place, (what, n, step, _) in enumerate(side_steps(first)):
                    if step == u:
                        act.wait_ge(side_loaded, 16 * (side_number(g, first, place) + 1))
                        if what == "b":
                            split_hi(b_sb[:, 0, n, :], side_in[:, :], side_hi, S_W)
                        else:
                            nc.scalar.activation(side_in[:, :], side_in[:, :], ACT.Identity, bias=quant_sb[:, 3:4],
                                                 scale=inv_scale[:, 1:2]).then_inc(ctx_affine, 1)

            def k_hi(b, use, bank):
                act.wait_ge(gen_done, use)
                split_hi(k_t[:, 0, b * SEQ:(b + 1) * SEQ], ps[:, bank, :], gen_hi, K_OUT)

            def v_hi(b, use, bank):
                act.wait_ge(gen_done, use)
                split_hi(v_sb[:, 0, b, :, :], ps[:, bank, :].rearrange("p (s d) -> p s d", s=QT), gen_hi, V_OUT)

            for n in range(LEAD):
                act.wait_ge(gen_done, 2 * DOWN + n + 1)
                split_hi(q_t[:, n, 0, :], ps[:, FIRST_Q[n], :], gen_hi, Q_OUT)
            for b in range(BATCH):
                k_hi(b, 2 * DOWN + LEAD + b + 1, FIRST_K[b])
            for b in range(BATCH):
                v_hi(b, 2 * DOWN + LEAD + BATCH + b + 1, FIRST_V[b])

            def group(g, last):
                first = isinstance(g, int) and g == 0
                uses = USES[last]

                def o_split(n):
                    act.wait_ge(pv_done, UNITS * g + n + 1)
                    if not first:
                        act.wait_ge(gen_done, PRE_USES + (g - 1) * PER_GROUP
                                    + USES[False][("wo", n // 4, WO_CHUNKS - 1)] + 1)
                    b = n % 2
                    split_hi(o_t[:, n // 2, 0, b * SEQ:(b + 1) * SEQ], ps[:, PV_BANK, :], o_hi, O_OUT)

                def pt_split(n, i):
                    width = sum(QT - k for k in PT_TURNS[i]) * P
                    at = PT_AT[PT_TURNS[i][0]]
                    act.wait_ge(pt_done, 3 * (UNITS * g + n) + i + 1)
                    if i == 0 and not (first and n < 2):
                        act.wait_ge(pv_done, UNITS * g + n - 1)
                    split_hi(prob_t[:, n % 2, 0, at:at + width], ps[:, PT_BANK[i], 0:width], pt_hi, 1.0)

                def exponentials(n):
                    act.wait_ge(scores_read, UNITS * g + n + 1)
                    for q in range(QT):
                        at = prob[:, n % 2, S_AT[q]:S_AT[q] + (q + 1) * P]
                        ins = nc.scalar.activation(at, at, ACT.Exp, bias=neg_max[:, n % 2, q:q + 1],
                                                   scale=SOFTMAX, accum_out=row_sum[:, n % 2, q:q + 1])
                    ins.then_inc(exp_done, 1)

                for u in range(STEPS):
                    short = last and UNITS - 2 <= u < UNITS
                    if u < UNITS and not short:
                        exponentials(u)
                    if u == UNITS and not last:
                        act.wait_ge(scores_done, 3 * UNITS * (g + 1))
                        k_hi(0, gen_number(g, last, ("k", 0)), GEN_BANK[uses[("k", 0)] % 2])
                    if 2 <= u < STEPS - 1:
                        o_split(u - 2)
                    if u == 6 and not last:
                        act.wait_ge(up_loaded, 16 * (g + 2))
                        act.wait_ge(gen_done, PRE_USES + g * PER_GROUP)
                        split_hi(up[:, 0, :, :, :], up_in[:, :, :, :], up_hi, S_W)
                    if 1 <= u <= UNITS:
                        pt_split(u - 1, 0)
                        pt_split(u - 1, 1)
                    if u < UNITS:
                        if u % 2 == 0:
                            if not (last and u >= 4):
                                wq_split(g, u // 2 + 2)
                        elif not (last and u == UNITS - 1):
                            wo_split(g, u // 2)
                    if short:
                        exponentials(u)
                    if ("q", u + LEAD) in uses and u < UNITS:
                        use = uses[("q", u + LEAD)]
                        act.wait_ge(gen_done, PRE_USES + g * PER_GROUP + use + 1)
                        n = u + LEAD
                        if not (first and n < 4):
                            act.wait_ge(scores_done, 3 * (UNITS * g + n - 3))
                        split_hi(q_t[:, n % 4, 0, :], ps[:, GEN_BANK[use % 2], :], gen_hi, Q_OUT)
                    if u == UNITS and not last:
                        k_hi(1, gen_number(g, last, ("k", 1)), GEN_BANK[uses[("k", 1)] % 2])
                    if 1 <= u <= UNITS:
                        pt_split(u - 1, 2)
                    if u == STEPS - 1:
                        o_split(u - 2)
                    if last and u == UNITS - 1:
                        wo_split(g, u // 2)
                    if last and 4 <= u < 8:
                        a_split(u - 4)
                    side_work(g, first, u)
                if not last:
                    for b in range(BATCH):
                        act.wait_ge(pv_done, UNITS * (g + 1))
                        v_hi(b, gen_number(g, last, ("v", b)), GEN_BANK[uses[("v", b)] % 2])

            group(0, False)
            with act.Fori(1, KV_HEADS - 1) as g:
                group(g, False)
            group(KV_HEADS - 1, True)

            def scale_rows(t):
                act.wait_ge(ln2_done, t + 1)
                at = hn[:, t % 2, :]
                nc.scalar.activation(at, at, ACT.Identity, bias=quant_sb[:, 1:2], scale=inv_scale[:, 0:1])\
                    .then_inc(x_affine, 1)

            for t in range(STEPS_AHEAD):
                scale_rows(t)
            for i in range(-1, TT + STEPS_AHEAD):
                if 0 <= i - 1 < TT:
                    t = i - 1
                    act.wait_ge(r_done, t + 1)
                    nc.scalar.activation(r_q[:, t % 2, :], ps[0:2 * ROUTER, SMALL_BANK, R_COL:R_COL + P], ACT.Copy,
                                         scale=ROUTER_OUT).then_inc(r_copied, 1)
                if 0 <= i + 1 < TT:
                    t = i + 1
                    act.wait_ge(x_turned, t + 1)
                    nc.scalar.activation(x_qt[:, t % 2, :], ps[:, TURN_BANK, :].bitcast(BF16), ACT.Copy).then_inc(x_qt_copied, 1)
                if 0 <= i - 1 < TT:
                    t = i - 1
                    act.wait_ge(s_done, t + 1)
                    nc.scalar.activation(score[:, t % 2, :], ps[:, SMALL_BANK, S_COL:S_COL + EXPERTS], ACT.Copy)\
                        .then_inc(s_copied, 1)
                    act.wait_ge(best_done, t + 1)
                    nc.scalar.activation(weight[:, t % 2, :], score[:, t % 2, :], ACT.Exp, bias=neg_best[:, t % 2:t % 2 + 1])\
                        .then_inc(weighted, 1)
                if 0 <= i < TT - STEPS_AHEAD:
                    scale_rows(i + STEPS_AHEAD)
                if 0 <= i < TT:
                    for j in range(2):
                        act.wait_ge(h3_turned, 2 * i + j + 1)
                        if j == 0 and i >= 2:
                            act.wait_ge(z_done, i - 1)
                        split_hi(h3_t[:, i % 2, 0, j * HALF:(j + 1) * HALF], ps[:, H_BANK[j], :], h3_hi, S_H)
                if 0 <= i - 1 < TT:
                    t = i - 1
                    act.wait_ge(z_turned, t + 1)
                    split_hi(z_t[:, t % 2, 0, :], ps[:, ZT_BANK, :], zt_hi, 1.0)

        @block.vector
        def _(dve):
            newtons = [0]

            def link(ins):
                newtons[0] += 1
                ins.then_inc(newton, 1)
                dve.wait_ge(newton, newtons[0])

            def split_lo(dst, src, hi, signal, scale):
                nc.vector.scalar_tensor_tensor(dst, src, scale, hi, ALU.mult, ALU.subtract).then_inc(signal, 1)

            variances = [0]

            def ln_stats(k, t):
                n = k * TT + t
                for j in range(2):
                    ins = nc.vector.bn_stats(stats[:, n, j, :], x_sb[:, t, j * HALF:(j + 1) * HALF])
                link(ins)
                link(nc.vector.bn_aggr(mean_var[:, n, :], stats[:, n, :, :].rearrange("p a b -> p (a b)")))
                nc.vector.tensor_scalar(var_eps[:, n:n + 1], mean_var[:, n, 1:2], EPS, None, ALU.add).then_inc(var_done, 1)
                variances[0] += 1
                return variances[0]

            def ln_apply(k, t, turn, dst, signal):
                n = k * TT + t
                dve.wait_ge(pow_done, turn)
                link(nc.vector.tensor_tensor(rstd1[:, 0, n:n + 1], rstd0[:, n:n + 1], rstd0[:, n:n + 1], ALU.mult))
                link(nc.vector.tensor_scalar(rstd1[:, 1, n:n + 1], rstd1[:, 0, n:n + 1], var_eps[:, n:n + 1], -0.5,
                                             ALU.mult, ALU.mult))
                link(nc.vector.scalar_tensor_tensor(rstd1[:, 2, n:n + 1], rstd1[:, 1, n:n + 1], 1.5, rstd0[:, n:n + 1],
                                                    ALU.add, ALU.mult))
                nc.vector.tensor_scalar(dst, x_sb[:, t, :], mean_var[:, n, 0:1], rstd1[:, 2, n:n + 1],
                                        ALU.subtract, ALU.mult).then_inc(signal, 1)

            def ln1_apply(t, turn):
                if t >= 2:
                    dve.wait_ge(ln_turned, 2 * (t - 1))
                ln_apply(0, t, turn, hn[:, t % 2, :], ln_done)

            def ln1_stats(t):
                dve.wait_ge(x_loaded[t], 16)
                return ln_stats(0, t)

            dve.wait_ge(consts, 6)
            nc.vector.tensor_copy(ident_b[:, :], ident[:, :]).then_inc(newton, 1)
            newtons[0] += 1
            def columns_lo(t):
                for j in range(2):
                    dve.wait_ge(ht_hi, 2 * t + j + 1)
                    split_lo(h_t[:, 1, 4 * j:4 * j + 4, t * P:(t + 1) * P],
                             ps[:, 2 * (t % 2) + j, :].rearrange("p (k n) -> p k n", k=4),
                             h_t[:, 0, 4 * j:4 * j + 4, t * P:(t + 1) * P], ht_lo, S_H)

            def latent_lo(b, hp):
                dve.wait_ge(gen_hi, b * DOWN + hp + 1)
                for half in range(2):
                    for j in range(2):
                        src, (hi, lo) = latent_views(b, hp, half, j)
                        ins = nc.vector.scalar_tensor_tensor(lo, src, LAT_OUT, hi, ALU.mult, ALU.subtract)
                ins.then_inc(gen_read, 1)

            turns = {t: ln1_stats(t) for t in range(2)}
            for t in range(2):
                ln1_apply(t, turns[t])
            turns[2] = ln1_stats(2)
            for t in range(TT):
                if t in (5, 6):
                    for hp in down_heads(t):
                        latent_lo(0, hp)
                columns_lo(t)
                if t + 2 < TT:
                    ln1_apply(t + 2, turns[t + 2])
                if t + 3 < TT:
                    turns[t + 3] = ln1_stats(t + 3)
            def wq_split(n, number):
                j = n % 2
                dve.wait_ge(wq_hi, number)
                split_lo(wq_sb[:, j, 1, :], wq_in[:, j, :], wq_sb[:, j, 0, :], wq_lo, S_W)

            for n in range(2):
                wq_split(n, n + 1)
            dve.wait_ge(up_hi, 1)
            split_lo(up[:, 1, :, :, :].rearrange("p a b c -> p (a b c)"), up_in[:, :, :, :].rearrange("p a b c -> p (a b c)"),
                     up[:, 0, :, :, :].rearrange("p a b c -> p (a b c)"), up_lo, S_W)
            dve.wait_ge(router_hi, 1)
            split_lo(router_sb[:, :, 1, :], router_in[:, :].rearrange("p (k r) -> p k r", r=ROUTER), router_sb[:, :, 0, :],
                     router_lo, S_W)
            dve.wait_ge(quant_loaded, 16)
            link(nc.vector.reciprocal(inv_scale[:, 0:1], quant_sb[:, 0:1]))
            link(nc.vector.reciprocal(inv_scale[:, 1:2], quant_sb[:, 2:3]))
            link(nc.vector.tensor_tensor(both_scales[:, :], quant_sb[:, 0:1], quant_sb[:, 2:3], ALU.mult))
            for n in range(2):
                link(nc.vector.tensor_scalar(shift[:, n:n + 1], quant_sb[:, 2 * n + 1:2 * n + 2], -1.0, CENTRE,
                                             ALU.mult, ALU.add))
            for n in range(2):
                link(nc.vector.tensor_scalar(shift_scaled[:, n:n + 1], shift[:, n:n + 1], both_scales[:, :], None, ALU.mult))
            link(nc.vector.tensor_scalar(shift_scaled[:, 2:3], shift_scaled[:, 0:1], shift[:, 1:2], float(CTX_K),
                                         ALU.mult, ALU.mult))

            for hp in range(DOWN):
                latent_lo(1, hp)

            def k_lo(b, bank):
                split_lo(k_t[:, 1, b * SEQ:(b + 1) * SEQ], ps[:, bank, :], k_t[:, 0, b * SEQ:(b + 1) * SEQ],
                         gen_read, K_OUT)

            def v_lo(b, bank):
                split_lo(v_sb[:, 1, b, :, :].rearrange("p s d -> p (s d)"), ps[:, bank, :],
                         v_sb[:, 0, b, :, :].rearrange("p s d -> p (s d)"), gen_read, V_OUT)

            def q_lo(n, bank):
                split_lo(q_t[:, n % 4, 1, :], ps[:, bank, :], q_t[:, n % 4, 0, :], gen_read, Q_OUT)

            for n in range(LEAD):
                dve.wait_ge(gen_hi, 2 * DOWN + n + 1)
                q_lo(n, FIRST_Q[n])
            for b in range(BATCH):
                dve.wait_ge(gen_hi, 2 * DOWN + LEAD + b + 1)
                k_lo(b, FIRST_K[b])
            for b in range(BATCH):
                dve.wait_ge(gen_hi, 2 * DOWN + LEAD + BATCH + b + 1)
                v_lo(b, FIRST_V[b])

            def group(g, last):
                first = isinstance(g, int) and g == 0
                uses = USES[last]

                def inverses(n):
                    dve.wait_ge(exp_done, UNITS * g + n + 1)
                    nc.vector.reciprocal(row_inv[:, n % 2, :], row_sum[:, n % 2, :]).then_inc(inv_done, 1)

                def wo_split(n):
                    dve.wait_ge(wo_hi, DOWN + 4 * g + n + 1)
                    split_lo(wo_sb[:, n, 1, :], wo_in[:, n % 2, :], wo_sb[:, n, 0, :], wo_lo, S_W)

                def wo_add(pair, c):
                    use = uses[("wo", pair, c)]
                    dve.wait_ge(gen_done, PRE_USES + g * PER_GROUP + use + 1)
                    t, half = c // 2, c % 2
                    at = x_sb[:, t, half * HALF:(half + 1) * HALF]
                    bank = c % LAST_BANKS if last and pair == 1 else GEN_BANK[use % 2]
                    nc.vector.scalar_tensor_tensor(at, ps[:, bank, :], WO_OUT, at,
                                                   ALU.mult, ALU.add).then_inc(gen_read, 1)

                def pt_split(n, i):
                    width = sum(QT - k for k in PT_TURNS[i]) * P
                    at = PT_AT[PT_TURNS[i][0]]
                    dve.wait_ge(pt_hi, 3 * (UNITS * g + n) + i + 1)
                    split_lo(prob_t[:, n % 2, 1, at:at + width], ps[:, PT_BANK[i], 0:width],
                             prob_t[:, n % 2, 0, at:at + width], pt_lo, 1.0)

                def o_split(n):
                    b = n % 2
                    dve.wait_ge(o_hi, UNITS * g + n + 1)
                    split_lo(o_t[:, n // 2, 1, b * SEQ:(b + 1) * SEQ], ps[:, PV_BANK, :],
                             o_t[:, n // 2, 0, b * SEQ:(b + 1) * SEQ], o_lo, O_OUT)

                for u in range(STEPS):
                    if u < UNITS:
                        if not (first and u < 2):
                            dve.wait_ge(pt_done, 3 * (UNITS * g + u - 1))
                        for i, tiles in enumerate(S_BANKS):
                            dve.wait_ge(scores_done, 3 * (UNITS * g + u) + i + 1)
                            dve.sem_inc(dve_passed)
                            for q in tiles:
                                width = (q + 1) * P
                                at = S_AT[q]
                                ins = nc.vector.tensor_tensor_reduce(
                                    prob[:, u % 2, at:at + width],
                                    ps[:, at // HALF, at % HALF:at % HALF + width], mask[:, SEQ - width:SEQ],
                                    1.0, MASKED, ALU.add, ALU.max, row_max[:, u % 2, q:q + 1])
                        ins.then_inc(max_done, 1)
                        dve.wait_ge(max_done, UNITS * g + u + 1)
                        nc.vector.tensor_scalar(neg_max[:, u % 2, :], row_max[:, u % 2, :], -SOFTMAX, None,
                                                ALU.mult).then_inc(scores_read, 1)
                    if u == UNITS:
                        if last:
                            wo_add(0, wo_span(u)[0])
                        else:
                            dve.wait_ge(gen_hi, hi_number(g, last, ("k", 0)))
                            k_lo(0, GEN_BANK[uses[("k", 0)] % 2])
                    if 2 <= u < STEPS - 1:
                        o_split(u - 2)
                    short = last and UNITS - 2 <= u < UNITS
                    if u < UNITS:
                        if not short:
                            inverses(u)
                    if u == 6 and not last:
                        dve.wait_ge(up_hi, g + 2)
                        split_lo(up[:, 1, :, :, :].rearrange("p a b c -> p (a b c)"),
                                 up_in[:, :, :, :].rearrange("p a b c -> p (a b c)"),
                                 up[:, 0, :, :, :].rearrange("p a b c -> p (a b c)"), up_lo, S_W)
                    if 1 <= u <= UNITS:
                        pt_split(u - 1, 0)
                        pt_split(u - 1, 1)
                    if u < UNITS:
                        if u % 2 == 0:
                            if not (last and u >= 4):
                                wq_split(u // 2 + 2, 4 * g + u // 2 + 3)
                        elif not (last and u == UNITS - 1):
                            wo_split(u // 2)
                    if ("q", u + LEAD) in uses and u < UNITS:
                        dve.wait_ge(gen_hi, hi_number(g, last, ("q", u + LEAD)))
                        q_lo(u + LEAD, GEN_BANK[uses[("q", u + LEAD)] % 2])
                    if u == UNITS and not last:
                        dve.wait_ge(gen_hi, hi_number(g, last, ("k", 1)))
                        k_lo(1, GEN_BANK[uses[("k", 1)] % 2])
                    if u >= UNITS - 2:
                        for place, c in enumerate(wo_span(u)[1 if last and u == UNITS else 0:]):
                            if short and place == 2:
                                inverses(u)
                            wo_add(0, c)
                    if 1 <= u <= UNITS:
                        pt_split(u - 1, 2)
                    if u == STEPS - 1:
                        o_split(u - 2)
                    if last and u == UNITS - 1:
                        wo_split(u // 2)
                    if last and 4 <= u < 8:
                        a_split(u - 4)
                    side_work(g, first, u)
                if not last:
                    for b in range(BATCH):
                        dve.wait_ge(gen_hi, hi_number(g, last, ("v", b)))
                        v_lo(b, GEN_BANK[uses[("v", b)] % 2])
                turns = {}
                for c in range(WO_CHUNKS):
                    wo_add(1, c)
                    if not last:
                        continue
                    for t in range(STEPS_AHEAD):
                        if c == 2 * t + 1:
                            dve.wait_ge(gen_read, gen_number(g, last, ("wo", 1, c)))
                            turns[t] = quantise_start(t)
                        if c == 4 + 3 * t:
                            quantise_apply(t, turns[t])
                        if c == 6 + 3 * t:
                            quantise_end(t)

            def a_split(n):
                dve.wait_ge(wq_hi, HEADS + n + 1)
                split_lo(a_sb[:, 1, n, :], wq_in[:, n % 2, :], a_sb[:, 0, n, :], wq_lo, S_W)

            def side_work(g, first, u):
                for what, n, _, step in side_steps(first):
                    if step != u:
                        continue
                    if what == "b":
                        dve.wait_ge(side_hi, n + 1)
                        split_lo(b_sb[:, 1, n, :], side_in[:, :], b_sb[:, 0, n, :], side_read, S_W)
                    else:
                        if not first:
                            dve.wait_ge(ctx_stored, 16 * (2 * g + n - 1))
                        dve.wait_ge(ctx_clipped, 2 * g + n + 1)
                        nc.vector.tensor_scalar(side_out[:, n, :], side_in[:, :], ROUND, -(ROUND + CENTRE),
                                                ALU.add, ALU.add).then_inc(side_read, 1)

            def quantise_start(t):
                turn = ln_stats(1, t)
                return turn

            def quantise_apply(t, turn):
                ln_apply(1, t, turn, hn[:, t % 2, :], ln2_done)

            def quantise_end(t):
                at = hn[:, t % 2, :]
                dve.wait_ge(x_affine, t + 1)
                link(nc.vector.tensor_scalar(at, at, QMAX, 0.0, ALU.min, ALU.max))
                if t >= 2:
                    dve.wait_ge(x_turned, t - 1)
                nc.vector.tensor_scalar(x_q[:, t % 2, :], at, ROUND, -(ROUND + CENTRE), ALU.add, ALU.add)\
                    .then_inc(x_rounded, 1)

            group(0, False)
            with dve.Fori(1, KV_HEADS - 1) as g:
                group(g, False)
            group(KV_HEADS - 1, True)

            def column_add(b):
                for j in range(2):
                    dve.wait_ge(column_done, 2 * b + j + 1)
                    nc.vector.tensor_scalar(column_term[:, b, j * HALF:(j + 1) * HALF], ps[:, COLUMN_BANK[b][j], :],
                                            shift_scaled[:, 0:1], shift_scaled[:, 2:3], ALU.mult, ALU.add)\
                        .then_inc(column_read, 1)

            for i in range(TT + STEPS_AHEAD):
                if i == 0:
                    column_add(0)
                if i < TT:
                    t, b = i, i // QT
                    dve.wait_ge(rows_done, t + 1)
                    nc.vector.tensor_scalar(row_term[:, t:t + 1], ps[:, SMALL_BANK, SUM_COL:SUM_COL + 1],
                                            shift_scaled[:, 1:2], None, ALU.mult).then_inc(row_read, 1)
                    dve.wait_ge(x_done, t + 1)
                    if t in (0, QT):
                        dve.wait_ge(column_read, 2 * (b + 1))
                    for j in range(2):
                        at = slice(j * HALF, (j + 1) * HALF)
                        ins = nc.vector.scalar_tensor_tensor(side_in[:, at], ps[:, X_BANK[j], :], both_scales[:, :],
                                                             column_term[:, b, at], ALU.mult, ALU.add)
                    ins.then_inc(x_added, 1)
                    dve.wait_ge(x_added, t + 1)
                    dve.wait_ge(row_read, t + 1)
                    link(nc.vector.scalar_tensor_tensor(x_sb[:, t, :], side_in[:, :], row_term[:, t:t + 1], x_sb[:, t, :],
                                                        ALU.add, ALU.add))
                    turn3 = ln_stats(2, t)
                if i + STEPS_AHEAD < TT:
                    turn2 = quantise_start(i + STEPS_AHEAD)
                if i < TT:
                    if i >= 2:
                        dve.wait_ge(h3_turned, 2 * (i - 1))
                    ln_apply(2, i, turn3, h3[i % 2], h3_done)
                    if i == 0:
                        column_add(1)
                if i + STEPS_AHEAD < TT:
                    quantise_apply(i + STEPS_AHEAD, turn2)
                if 0 <= i - 1 < TT:
                    t = i - 1
                    dve.wait_ge(s_copied, t + 1)
                    link(nc.vector.max(best[:, t % 2, 0, :], score[:, t % 2, :]))
                    nc.vector.tensor_scalar(neg_best[:, t % 2:t % 2 + 1], best[:, t % 2, 0, 0:1], -1.0, None, ALU.mult)\
                        .then_inc(best_done, 1)
                    link(nc.vector.match_replace(left[:, t % 2, 0, :], best[:, t % 2, 0, :], score[:, t % 2, :], TAKEN))
                    link(nc.vector.max(best[:, t % 2, 1, :], left[:, t % 2, 0, :]))
                    link(nc.vector.match_replace(left[:, t % 2, 1, :], best[:, t % 2, 1, :], left[:, t % 2, 0, :], TAKEN))
                    dve.wait_ge(weighted, t + 1)
                    link(nc.vector.scalar_tensor_tensor(gate[:, t % 2, :], left[:, t % 2, 1, :], TAKEN, weight[:, t % 2, :],
                                                        ALU.is_equal, ALU.mult, accum_out=gate_sum[:, t:t + 1]))
                    dve.wait_ge(z_done, t + 1)
                    if t >= 1:
                        dve.wait_ge(z_turned, t)
                    nc.vector.scalar_tensor_tensor(
                        gated.rearrange("p (e r) -> p e r", r=RANK),
                        ps[:, Z_BANK, :].rearrange("p (e r) -> p e r", r=RANK), Z_OUT,
                        gate[:, t % 2, :].unsqueeze(2).to_broadcast([P, EXPERTS, RANK]), ALU.mult, ALU.mult)\
                        .then_inc(z_gated, 1)
                    link(nc.vector.reciprocal(gate_inv[:, t:t + 1], gate_sum[:, t:t + 1]))
                    link(nc.vector.tensor_scalar(gate_scale[:, t:t + 1], gate_inv[:, t:t + 1], FFN_OUT, None, ALU.mult))
                if i + STEPS_AHEAD < TT:
                    quantise_end(i + STEPS_AHEAD)
                if 0 <= i - 2 < TT:
                    t = i - 2
                    for j in range(2):
                        at = slice(j * HALF, (j + 1) * HALF)
                        dve.wait_ge(out_full, 2 * t + j + 1)
                        nc.vector.scalar_tensor_tensor(x_sb[:, t, at], ps[:, X_BANK[j], :], gate_scale[:, t:t + 1],
                                                       x_sb[:, t, at], ALU.mult, ALU.add).then_inc(out_done, 1)
                if i < TT:
                    for j in range(2):
                        at = slice(j * HALF, (j + 1) * HALF)
                        dve.wait_ge(h3_hi, 2 * i + j + 1)
                        split_lo(h3_t[:, i % 2, 1, at], ps[:, H_BANK[j], :], h3_t[:, i % 2, 0, at], h3_lo, S_H)
                if 0 <= i - 1 < TT:
                    t = i - 1
                    dve.wait_ge(zt_hi, t + 1)
                    split_lo(z_t[:, t % 2, 1, :], ps[:, ZT_BANK, :], z_t[:, t % 2, 0, :], zt_lo, 1.0)

        @block.tensor
        def _(pe):
            PASSES = ((0, 0), (0, 1), (1, 0))

            def split_product(out_, pairs, start=True, stop=True):
                n = 0
                for lhs, rhs in pairs:
                    for i, j in PASSES:
                        ins = nc.tensor.matmul(out_, lhs(i), rhs(j), start=start and n == 0,
                                               stop=stop and n == 3 * len(pairs) - 1)
                        n += 1
                return ins

            pe.wait_ge(consts, 6)
            def columns(t):
                pe.wait_ge(ln_done, t + 1)
                for j in range(2):
                    if t >= 2:
                        pe.wait_ge(ht_lo, 2 * (t - 2) + j + 1)
                    for k in range(4):
                        at = (4 * j + k) * P
                        ins = nc.tensor.transpose(ps[:, 2 * (t % 2) + j, k * P:(k + 1) * P],
                                                  hn[:, t % 2, at:at + P], ident[:, :])
                    ins.then_inc(ln_turned, 1)

            for t in range(2):
                columns(t)
            for pair in range(PAIRS):
                b, part = pair // 2, pair % 2
                at = pair * 2 * P
                for hp in range(DOWN):
                    if hp < 2 and 2 * pair + 2 + hp < TT:
                        columns(2 * pair + 2 + hp)
                    if hp == 0:
                        pe.wait_ge(ht_lo, 4 * (pair + 1))
                    if pair == 0:
                        pe.wait_ge(wo_lo, hp + 1)
                    if b == 1 and part == 0:
                        pe.wait_ge(gen_read, hp + 1)
                    ins = split_product(ps[:, DOWN_BANK[hp], part * 2 * P:(part + 1) * 2 * P],
                                        [(lambda i, k=k: wo_sb[:, hp, i, k * P:(k + 1) * P],
                                          lambda j, k=k: h_t[:, j, k, at:at + 2 * P]) for k in range(KT)])
                    if part == 1:
                        ins.then_inc(gen_done, 1)

            def k_product(b, bank):
                return split_product(ps[:, bank, :],
                                     [(lambda i, c=c: up[:, i, 0, c, :],
                                       lambda j, c=c: lat[:, j, c, b * SEQ:(b + 1) * SEQ]) for c in range(2)])

            def v_product(b, bank):
                for s in range(QT):
                    at = b * SEQ + s * P
                    ins = split_product(ps[:, bank, s * P:(s + 1) * P],
                                        [(lambda i, c=c: lat[:, i, 2 + c, at:at + P],
                                          lambda j, c=c: up[:, j, 1, c, :]) for c in range(2)])
                return ins

            def q_product(n, bank, part):
                b, j2 = n % 2, (n // 2) % 2
                lo, hi = (0, KT // 2) if part == 0 else (KT // 2, KT)
                return split_product(ps[:, bank, :],
                                     [(lambda i, k=k: wq_sb[:, j2, i, k * P:(k + 1) * P],
                                       lambda j, k=k: h_t[:, j, k, b * SEQ:(b + 1) * SEQ]) for k in range(lo, hi)],
                                     start=part == 0, stop=part == 1)

            pe.wait_ge(wq_lo, 1)
            pe.wait_ge(ht_lo, 2 * TT)
            for n in range(LEAD):
                q_product(n, FIRST_Q[n], 0)
                q_product(n, FIRST_Q[n], 1).then_inc(gen_done, 1)
            pe.wait_ge(up_lo, 1)
            pe.wait_ge(gen_read, 2 * DOWN)
            for b in range(BATCH):
                k_product(b, FIRST_K[b]).then_inc(gen_done, 1)
            for b in range(BATCH):
                v_product(b, FIRST_V[b]).then_inc(gen_done, 1)

            def group(g, last):
                first = isinstance(g, int) and g == 0
                uses = USES[last]
                base = PRE_USES + g * PER_GROUP

                def bank_free(what):
                    pe.wait_ge(gen_read, base + uses[what] - 1)
                    return GEN_BANK[uses[what] % 2]

                def wo_chunk(pair, c):
                    if last and pair == 1:
                        pe.wait_ge(gen_read, base + uses[("wo", 1, max(c - LAST_BANKS + 1, 0))])
                        bank = c % LAST_BANKS
                    else:
                        bank = bank_free(("wo", pair, c))
                    if c == 0:
                        pe.wait_ge(wo_lo, DOWN + 4 * g + 2 * pair + 2)
                    if c in (0, WO_CHUNKS // 2):
                        pe.wait_ge(o_lo, UNITS * g + 4 * pair + 3 + 2 * c // WO_CHUNKS)
                    if last and pair == 1 and bank == PV_BANK:
                        pe.wait_ge(o_lo, UNITS * (g + 1))
                    t, half = c // 2, c % 2
                    split_product(ps[:, bank, :],
                                  [(lambda i, n=n: o_t[:, n, i, t * P:(t + 1) * P],
                                    lambda j, n=n: wo_sb[:, n, j, half * HALF:(half + 1) * HALF])
                                   for n in (2 * pair, 2 * pair + 1)]).then_inc(gen_done, 1)

                def turn(n, i):
                    if not (first and n == 0 and i < 2):
                        pe.wait_ge(pt_lo, 3 * (UNITS * g + n) + (0, -1, 1)[i])
                    at = 0
                    for k in PT_TURNS[i]:
                        for q in range(k, QT):
                            ins = nc.tensor.transpose(
                                ps[:, PT_BANK[i], at:at + P],
                                prob[:, n % 2, S_AT[q] + k * P:S_AT[q] + (k + 1) * P], ident[:, :])
                            at += P
                    ins.then_inc(pt_done, 1)

                def outputs(n):
                    pe.wait_ge(pt_lo, 3 * (UNITS * g + n) + 2)
                    if n == 0 and not first:
                        pe.wait_ge(gen_read, PRE_USES + (g - 1) * PER_GROUP + USES[False][("v", 1)] + 1)
                    if not (first and n == 0):
                        pe.wait_ge(o_lo, UNITS * g + n)
                    for k in PT_TURNS[0] + PT_TURNS[1] + PT_TURNS[2]:
                        if k == PT_TURNS[2][0]:
                            pe.wait_ge(pt_lo, 3 * (UNITS * g + n + 1))
                        width = (QT - k) * P
                        ins = split_product(ps[:, PV_BANK, k * P:SEQ],
                                            [(lambda i: v_sb[:, i, n % 2, k, :],
                                              lambda j: prob_t[:, n % 2, j, PT_AT[k]:PT_AT[k] + width])],
                                            start=k == 0, stop=k == PT_TURNS[2][0])
                    ins.then_inc(pv_done, 1)

                for u in range(STEPS):
                    if u < UNITS:
                        b = u % 2
                        if u == 0:
                            if first:
                                pe.wait_ge(gen_read, 2 * DOWN + LEAD + BATCH)
                            else:
                                pe.wait_ge(gen_read, PRE_USES + (g - 1) * PER_GROUP + USES[False][("k", 1)] + 1)
                        elif u == 1:
                            if first:
                                pe.wait_ge(gen_read, PRE_USES)
                        else:
                            pe.wait_ge(gen_read, base + uses[("q", u)] + 1)
                        if not (first and u == 0):
                            pe.wait_ge(scores_read, UNITS * g + u)
                        for tiles in S_BANKS:
                            for q in tiles:
                                at, width = S_AT[q], (q + 1) * P
                                ins = split_product(ps[:, at // HALF, at % HALF:at % HALF + width],
                                                    [(lambda i: q_t[:, u % 4, i, q * P:(q + 1) * P],
                                                      lambda j: k_t[:, j, b * SEQ:b * SEQ + width])])
                            ins.then_inc(scores_done, 1)
                    if u == UNITS:
                        if last:
                            wo_chunk(0, wo_span(u)[0])
                        else:
                            pe.wait_ge(up_lo, g + 2)
                            k_product(0, bank_free(("k", 0))).then_inc(gen_done, 1)
                    if 2 <= u < STEPS - 1:
                        outputs(u - 2)
                    q_what = ("q", u + LEAD)
                    has_q = q_what in uses and u < UNITS
                    if has_q:
                        bank = bank_free(q_what)
                        if u % 2 == 0:
                            pe.wait_ge(wq_lo, 4 * g + (u + LEAD) // 2 + 1)
                        q_product(u + LEAD, bank, 0)
                    if 1 <= u <= UNITS:
                        pe.wait_ge(prob_normed, UNITS * g + u)
                        turn(u - 1, 0)
                        turn(u - 1, 1)
                    if has_q:
                        q_product(u + LEAD, bank, 1).then_inc(gen_done, 1)
                    if u == UNITS and not last:
                        k_product(1, bank_free(("k", 1))).then_inc(gen_done, 1)
                    if u >= UNITS - 2:
                        for c in wo_span(u)[1 if last and u == UNITS else 0:]:
                            wo_chunk(0, c)
                    if 1 <= u <= UNITS:
                        turn(u - 1, 2)
                    if u == STEPS - 1:
                        outputs(u - 2)
                if not last:
                    for b in range(BATCH):
                        v_product(b, bank_free(("v", b))).then_inc(gen_done, 1)
                for c in range(WO_CHUNKS):
                    wo_chunk(1, c)

            group(0, False)
            with pe.Fori(1, KV_HEADS - 1) as g:
                group(g, False)
            group(KV_HEADS - 1, True)

            def column_sums(b):
                pe.wait_ge(ctx_loaded[b], 16)
                for j in range(2):
                    for k in range(KT):
                        ins = nc.tensor.matmul(ps[:, COLUMN_BANK[b][j], :], ones[:, :], ctx_q[:, b, k, j * HALF:(j + 1) * HALF],
                                               start=k == 0, stop=k == KT - 1)
                    ins.then_inc(column_done, 1)

            for i in range(-1, TT + STEPS_AHEAD):
                if i == 0:
                    pe.wait_ge(gen_read, gen_number(KV_HEADS - 1, True, ("wo", 1, LAST_BANKS + X_BANK[1])))
                    column_sums(0)
                if 0 <= i < TT:
                    t, b = i, i // QT
                    pe.wait_ge(x_qt_copied, t + 1)
                    if t == 0:
                        pe.wait_ge(gen_read, gen_number(KV_HEADS - 1, True, ("wo", 1, WO_CHUNKS - 1)))
                    if t >= 2:
                        pe.wait_ge(s_copied, t - 1)
                    for k in range(KT):
                        ins = nc.tensor.matmul(ps[:, SMALL_BANK, SUM_COL:SUM_COL + 1], x_qt[:, t % 2, k * P:(k + 1) * P],
                                               ones[:, 0:1], start=k == 0, stop=k == KT - 1)
                    ins.then_inc(rows_done, 1)
                    if t == 0:
                        pe.wait_ge(column_read, 2)
                    for j in range(2):
                        if t >= 3:
                            pe.wait_ge(out_done, 2 * (t - 3) + j + 1)
                        for k in range(KT):
                            ins = nc.tensor.matmul(ps[:, X_BANK[j], :], x_qt[:, t % 2, k * P:(k + 1) * P],
                                                   ctx_q[:, b, k, j * HALF:(j + 1) * HALF], start=k == 0, stop=k == KT - 1)
                    ins.then_inc(x_done, 1)
                    if t == 0:
                        column_sums(1)
                if 0 <= i - 1 < TT:
                    t = i - 1
                    pe.wait_ge(h3_lo, 2 * t + 2)
                    if t == 0:
                        pe.wait_ge(router_lo, 1)
                        pe.wait_ge(wq_lo, HEADS + KT // 2)
                    pe.wait_ge(row_read, min(t + 2, TT))
                    for n in range(2 * KT):
                        k, part = n // 2, n % 2
                        ins = nc.tensor.matmul(ps[0:2 * ROUTER, SMALL_BANK, R_COL:R_COL + P],
                                               router_sb[:, k, :, :].rearrange("p a r -> p (a r)"),
                                               h3_t[:, t % 2, part, k * P:(k + 1) * P],
                                               start=n == 0, stop=n == 2 * KT - 1)
                    ins.then_inc(r_done, 1)
                    if t == 0:
                        pe.wait_ge(column_read, 4)
                    if t >= 1:
                        pe.wait_ge(z_gated, t)
                    split_product(ps[:, Z_BANK, :],
                                  [(lambda n, k=k: h3_t[:, t % 2, n, k * P:(k + 1) * P],
                                    lambda m, k=k: a_sb[:, m, k // 2, (k % 2) * HALF:(k % 2 + 1) * HALF]) for k in range(KT)]
                                  ).then_inc(z_done, 1)
                if 0 <= i + 1 < TT:
                    t = i + 1
                    pe.wait_ge(x_rounded, t + 1)
                    if t == 0:
                        pe.wait_ge(gen_read, gen_number(KV_HEADS - 1, True, ("wo", 1, LAST_BANKS + TURN_BANK)))
                    if t >= 1:
                        pe.wait_ge(x_qt_copied, t)
                    if t >= 2:
                        pe.wait_ge(x_done, t - 1)
                    for k in range(KT):
                        ins = nc.tensor.transpose(ps[:, TURN_BANK, :].bitcast(BF16)[:, k * P:(k + 1) * P],
                                                  x_q[:, t % 2, k * P:(k + 1) * P], ident_b[:, :])
                    ins.then_inc(x_turned, 1)
                if 0 <= i - 1 < TT:
                    t = i - 1
                    pe.wait_ge(r_copied, t + 1)
                    nc.tensor.matmul(ps[:, SMALL_BANK, S_COL:S_COL + EXPERTS], r_q[:, t % 2, :], keys_sb[:, :],
                                     start=True, stop=True).then_inc(s_done, 1)
                if 0 <= i - 2 < TT:
                    t = i - 2
                    pe.wait_ge(zt_lo, t + 1)
                    if t == 0:
                        pe.wait_ge(side_read, BT)
                    pe.wait_ge(x_added, min(i + 1, TT))
                    for j in range(2):
                        split_product(ps[:, X_BANK[j], :],
                                      [(lambda n, k=k: z_t[:, t % 2, n, k * P:(k + 1) * P],
                                        lambda m, k=k: b_sb[:, m, k, j * HALF:(j + 1) * HALF]) for k in range(BT)]
                                      ).then_inc(out_full, 1)
                if 0 <= i < TT:
                    pe.wait_ge(h3_done, i + 1)
                    for j in range(2):
                        if i >= 1:
                            pe.wait_ge(h3_lo, 2 * (i - 1) + j + 1)
                        for k in range(4):
                            at = j * HALF + k * P
                            ins = nc.tensor.transpose(ps[:, H_BANK[j], k * P:(k + 1) * P], h3[i % 2][:, at:at + P],
                                                      ident[:, :])
                        ins.then_inc(h3_turned, 1)
                if 0 <= i - 1 < TT:
                    t = i - 1
                    pe.wait_ge(z_gated, t + 1)
                    if t >= 1:
                        pe.wait_ge(zt_lo, t)
                    for k in range(BT):
                        ins = nc.tensor.transpose(ps[:, ZT_BANK, k * P:(k + 1) * P], gated[:, k * P:(k + 1) * P], ident[:, :])
                    ins.then_inc(z_turned, 1)


def layouts(np, x, ctx_4096, Wq, Wk_down, Wv_down, Wk_up, Wv_up, Wo, A_w, B_w, Wq_w, keys):
    c = np.ascontiguousarray
    down = np.stack([Wk_down.reshape(KV_HEADS, LAT, DIM), Wv_down.reshape(KV_HEADS, LAT, DIM)], 1)
    down = down.reshape(DOWN, P, KT, P).transpose(0, 3, 2, 1)
    ups = [w.reshape(KV_HEADS, HD, 2, P).transpose(0, 3, 2, 1) for w in (Wk_up, Wv_up)]
    return {
        "x": c(x.reshape(TT, P, DIM)),
        "ctx": c(ctx_4096.reshape(CTX_CHUNKS, P, CTX_N)),
        "wq": c(Wq.reshape(HEADS, HD, KT, P).transpose(0, 3, 2, 1).reshape(HEADS, P, KT * HD)),
        "wdown": c(down.reshape(DOWN, P, KT * P)),
        "wup": c(np.stack(ups, 2)),
        "wo": c(Wo.T.reshape(HEADS, HD, DIM)),
        "a_w": c(A_w.T.reshape(KT, P, BOTTLE).transpose(1, 0, 2).reshape(P, KT // 2, DIM)),
        "b_w": c(B_w.T.reshape(BT, P, DIM).transpose(1, 0, 2)),
        "router_w": c(Wq_w.T.reshape(KT, P, ROUTER).transpose(1, 0, 2).reshape(P, KT * ROUTER)),
        "keys": c(keys.T),
    }


def kernel(**inputs):
    import numpy as np
    import concourse.bacc as bacc
    from concourse.bass_utils import run_bass_kernel_spmd

    a = {k: np.asarray(v) for k, v in inputs.items()}
    arrays = layouts(np, a["x"], a["ctx_4096"],
                     *(a["L0_attn_" + k] for k in ("Wq", "Wk_down", "Wv_down", "Wk_up", "Wv_up", "Wo")),
                     *(a["L0_ffn_" + k] for k in ("A_w", "B_w", "Wq_w", "keys")))
    arrays["quant"] = np.stack([a["L0_xattn_" + k].reshape(()) for k in ("x1_scale", "x1_zp", "x2_scale", "x2_zp")]).reshape(1, 4)
    nc = bacc.Bacc("TRN2", target_bir_lowering=False, num_devices=1)
    aps = {k: nc.dram_tensor("in_" + k, v.shape, mybir.dt.from_np(v.dtype), kind="ExternalInput").ap()
           for k, v in arrays.items()}
    ctx_whole = nc.dram_tensor("ctx_quantised", (CTX_CHUNKS, P, CTX_N), BF16, kind="Internal").ap()
    out = nc.dram_tensor("out", (TT, P, DIM), F32, kind="ExternalOutput").ap()
    decoder_layer(nc, aps["x"], aps["ctx"], aps["wq"], aps["wdown"], aps["wup"], aps["wo"], aps["a_w"], aps["b_w"],
                  aps["router_w"], aps["keys"], aps["quant"], ctx_whole, out)
    r = run_bass_kernel_spmd(nc, [{"in_" + k: v for k, v in arrays.items()}], core_ids=[0])
    return r.results[0]["out"].reshape(BATCH, SEQ, DIM)
```
